# Optimizing a Trainium2 kernel written in Bass

```python
import numpy as np
import jax
import jax.numpy as jnp

def _softmax(x, axis=-1):
    return jax.nn.softmax(x, axis=axis)

def _gelu(x):
    return jax.nn.gelu(x, approximate=True)

def _silu(x):
    return jax.nn.silu(x)

def _sigmoid(x):
    return jax.nn.sigmoid(x)

def _layernorm(x, axis=-1, eps=1e-05):
    m = jnp.mean(x, axis=axis, keepdims=True)
    v = jnp.var(x, axis=axis, keepdims=True)
    return (x - m) / jnp.sqrt(v + eps)

def _scatter_add(tgt, idx, src, axis=0):
    return tgt.at[idx].add(src)

def _segment_sum(src, seg, n):
    return jax.ops.segment_sum(src, seg, n)
kernel_name = 'mk_gnn_ffn_d1_gnn_r8_44ee37'

def setup_inputs(seed: int=0):
    np.random.seed(seed)
    _w = jnp.asarray

    def _rec_inputs():
        import jax
        import jax.numpy as jnp
        _gk = jax.random.key(seed)
        x = -0.0002117 + 1 * jax.random.normal(jax.random.fold_in(_gk, 1), (3125, 1024), jnp.float32)
        _s = jax.random.randint(jax.random.fold_in(_gk, 2), (25000,), 0, 3125, jnp.int32)
        _d = jax.random.randint(jax.random.fold_in(_gk, 3), (25000,), 0, 3125, jnp.int32)
        _loop = jnp.arange(3125, dtype=jnp.int32)
        src = jnp.concatenate([_s, _d, _loop])
        dst = jnp.concatenate([_d, _s, _loop])
        _o = jnp.argsort(dst, stable=True)
        src = src[_o]
        dst = dst[_o]
        return (x, src, dst)
    x, src, dst = _rec_inputs()

    def _L0_gnn_setup():
        import jax, jax.numpy as jnp
        import numpy as np
        N = 3125
        E = 50000
        H = 4
        C = 256
        D_IN = 1024
        NEG_SLOPE = 0.2
        key = jax.random.key(seed)
        k1, k2, k3, k4, k5, k6 = jax.random.split(key, 6)
        x = jax.random.normal(k1, (N, D_IN), dtype=jnp.float32)
        edge_index = jax.random.randint(k2, (2, E), 0, N, dtype=jnp.int64)
        scale = 1.0 / np.sqrt(D_IN)
        W = jax.random.normal(k3, (D_IN, H * C), dtype=jnp.float32) * scale
        att_src = jax.random.normal(k4, (H, C), dtype=jnp.float32) * 0.1
        att_dst = jax.random.normal(k5, (H, C), dtype=jnp.float32) * 0.1
        bias = jax.random.normal(k6, (H * C,), dtype=jnp.float32) * 0.01
        return {'x': x, 'edge_index': edge_index, 'W': W, 'att_src': att_src, 'att_dst': att_dst, 'bias': bias}
    _L0_gnn_all = _L0_gnn_setup()
    _L0_gnn_in = {k: v for k, v in _L0_gnn_all.items() if k in ('W', 'att_src', 'att_dst', 'bias')}
    del _L0_gnn_all

    def _L0_ffn_setup():
        import jax, jax.numpy as jnp
        import numpy as np
        B, T, D_MODEL = (4, 256, 1024)
        N_EXPERTS, TOP_K, D_EXPERT = (6, 2, 512)
        QUANT_TEMP = 0.3
        _ANCHOR_IDS = [63, 6, 0, 18, 45, 27]

        def _q6_idx_to_vertex(idx):
            bits = [idx >> 5 - b & 1 for b in range(6)]
            return [2.0 * b - 1.0 for b in bits]

        def _anchors():
            return jnp.asarray(np.array([_q6_idx_to_vertex(i) for i in _ANCHOR_IDS], dtype=np.float32))

        def _router(x, proj_w, anchors, routing_temp):
            z = jnp.einsum('btd,ed->bte', x, proj_w)
            q = jnp.tanh(z / QUANT_TEMP)
            dot = jnp.einsum('btd,ed->bte', q, anchors)
            hamming = (6.0 - dot) * 0.5
            logits = -hamming / jnp.clip(routing_temp, 0.1)
            topk_logits, topk_idx = jax.lax.top_k(logits, TOP_K)
            topk_w = jax.nn.softmax(topk_logits, axis=-1)
            onehot = jax.nn.one_hot(topk_idx, N_EXPERTS, dtype=x.dtype)
            expert_weights = jnp.einsum('btke,btk->bte', onehot, topk_w)
            return (expert_weights, q)
        key = jax.random.key(seed)
        k_x, k_p, k_w1, k_w2 = jax.random.split(key, 4)
        x = jax.random.normal(k_x, (B, T, D_MODEL), dtype=jnp.float32)
        proj_w = jax.random.normal(k_p, (6, D_MODEL), dtype=jnp.float32) * 0.02
        anchors = _anchors()
        routing_temp = jnp.array(1.0, dtype=jnp.float32)
        s1 = 1.0 / np.sqrt(D_MODEL)
        s2 = 1.0 / np.sqrt(D_EXPERT)
        w1 = jax.random.uniform(k_w1, (N_EXPERTS, D_MODEL, D_EXPERT), jnp.float32, -s1, s1)
        w2 = jax.random.uniform(k_w2, (N_EXPERTS, D_EXPERT, D_MODEL), jnp.float32, -s2, s2)
        return {'x': x, 'proj_w': proj_w, 'anchors': anchors, 'routing_temp': routing_temp, 'w1': w1, 'w2': w2}
    _L0_ffn_all = _L0_ffn_setup()
    _L0_ffn_in = {k: v for k, v in _L0_ffn_all.items() if k in ('proj_w', 'anchors', 'routing_temp', 'w1', 'w2')}
    del _L0_ffn_all
    return {'x': x, 'src': src, 'dst': dst, 'L0_gnn_W': _L0_gnn_in['W'], 'L0_gnn_att_src': _L0_gnn_in['att_src'], 'L0_gnn_att_dst': _L0_gnn_in['att_dst'], 'L0_gnn_bias': _L0_gnn_in['bias'], 'L0_ffn_proj_w': _L0_ffn_in['proj_w'], 'L0_ffn_anchors': _L0_ffn_in['anchors'], 'L0_ffn_routing_temp': _L0_ffn_in['routing_temp'], 'L0_ffn_w1': _L0_ffn_in['w1'], 'L0_ffn_w2': _L0_ffn_in['w2']}

def reference(x, src, dst, L0_gnn_W, L0_gnn_att_src, L0_gnn_att_dst, L0_gnn_bias, L0_ffn_proj_w, L0_ffn_anchors, L0_ffn_routing_temp, L0_ffn_w1, L0_ffn_w2):
    import jax
    import jax.numpy as jnp

    def _L0_gnn_ref(x, edge_index, W, att_src, att_dst, bias):
        import jax, jax.numpy as jnp
        import numpy as np
        N = 3125
        E = 50000
        H = 4
        C = 256
        D_IN = 1024
        NEG_SLOPE = 0.2
        xp = (x @ W).reshape(N, H, C)
        a_src = jnp.einsum('nhc,hc->nh', xp, att_src)
        a_dst = jnp.einsum('nhc,hc->nh', xp, att_dst)
        loops = jnp.arange(N, dtype=edge_index.dtype)
        src = jnp.concatenate([edge_index[0], loops])
        dst = jnp.concatenate([edge_index[1], loops])
        e = jax.nn.leaky_relu(a_src[src] + a_dst[dst], NEG_SLOPE)
        m = jax.ops.segment_max(e, dst, num_segments=N)
        ee = jnp.exp(e - m[dst])
        z = jax.ops.segment_sum(ee, dst, num_segments=N)
        alpha = ee / z[dst]
        msgs = xp[src] * alpha[:, :, None]
        out = jax.ops.segment_sum(msgs, dst, num_segments=N)
        out = out.reshape(N, H * C) + bias
        return jax.nn.relu(out)

    def _L0_ffn_ref(x, proj_w, anchors, routing_temp, w1, w2):
        import jax, jax.numpy as jnp
        import numpy as np
        B, T, D_MODEL = (4, 256, 1024)
        N_EXPERTS, TOP_K, D_EXPERT = (6, 2, 512)
        QUANT_TEMP = 0.3
        _ANCHOR_IDS = [63, 6, 0, 18, 45, 27]

        def _q6_idx_to_vertex(idx):
            bits = [idx >> 5 - b & 1 for b in range(6)]
            return [2.0 * b - 1.0 for b in bits]

        def _anchors():
            return jnp.asarray(np.array([_q6_idx_to_vertex(i) for i in _ANCHOR_IDS], dtype=np.float32))

        def _router(x, proj_w, anchors, routing_temp):
            z = jnp.einsum('btd,ed->bte', x, proj_w)
            q = jnp.tanh(z / QUANT_TEMP)
            dot = jnp.einsum('btd,ed->bte', q, anchors)
            hamming = (6.0 - dot) * 0.5
            logits = -hamming / jnp.clip(routing_temp, 0.1)
            topk_logits, topk_idx = jax.lax.top_k(logits, TOP_K)
            topk_w = jax.nn.softmax(topk_logits, axis=-1)
            onehot = jax.nn.one_hot(topk_idx, N_EXPERTS, dtype=x.dtype)
            expert_weights = jnp.einsum('btke,btk->bte', onehot, topk_w)
            return (expert_weights, q)
        expert_weights, q = _router(x, proj_w, anchors, routing_temp)
        h = jax.nn.gelu(jnp.einsum('btd,edh->bteh', x, w1))
        out = jnp.einsum('bteh,ehd,bte->btd', h, w2, expert_weights)
        return out
    edge_index = jnp.stack([src, dst])
    x = x + _L0_gnn_ref(_layernorm(x, axis=-1), edge_index, L0_gnn_W, L0_gnn_att_src, L0_gnn_att_dst, L0_gnn_bias)
    x = x + _L0_ffn_ref(_layernorm(x, axis=-1)[None], L0_ffn_proj_w, L0_ffn_anchors, L0_ffn_routing_temp, L0_ffn_w1, L0_ffn_w2)[0]
    return x

_drawn_inputs = setup_inputs


def setup_inputs(seed=0):
    import zlib

    import numpy as np

    out = dict(_drawn_inputs(seed))
    spreads = {}
    factors = {'L0_gnn_bias': 5.553}
    for name, (base, spread) in spreads.items():
        noise = np.random.default_rng([zlib.crc32(name.encode()), seed]).standard_normal(out[name].shape)
        drawn = base * np.exp(spread * noise) if base else spread * noise
        out[name] = jnp.asarray(drawn.astype(out[name].dtype))
    for name, factor in factors.items():
        out[name] = (out[name] * factor).astype(out[name].dtype)
    return out
```

```python
from contextlib import ExitStack

import numpy as np

import concourse.bass as bass
from concourse import mybir

P = 128
N = 3125
D = 1024
H, C = 4, 256
NE, DH = 6, 512
E = 53125
NT = -(-N // P)
NP = NT * P
KD = D // P
KH = DH // P
EC = 416
EP = P * EC
EPAD = P
NO_NODE = 4095
LAST_SLOT = (E + NT * (P - 1)) // P
U = 8
S = -(-LAST_SLOT // U) * U
AHEAD = 2
SC = 4
S2 = (2 * NP + NE * (P - 1)) // P
S2 += S2 % 2
CREDIT = 2
BIG = 1.0e30
EPS = 1e-5
SLOPE = 0.2
QUANT_TEMP = 0.3
SKIP = 1 << 24

F32 = mybir.dt.float32
BF16 = mybir.dt.bfloat16
I32 = mybir.dt.int32
ALU = mybir.AluOpType
ACT = mybir.ActivationFunctionType
X = mybir.AxisListType.X
ds = bass.ds

assert P * SC >= S + AHEAD and EC * P >= E and EC % 16 == 0


class Chain:

    def __init__(self, eng, sem):
        self.eng, self.sem, self.n, self.base = eng, sem, 0, 0

    def __call__(self, ins):
        ins.then_inc(self.sem, 1)
        self.n += 1
        self.eng.wait_ge(self.sem, self.base + self.n)

    def loop(self, i, per, body):
        start = self.n
        self.base, self.n = i * per + start, 0
        body()
        assert self.n == per
        self.base, self.n = 0, start

    def passed(self, steps):
        self.n += steps


def tiles(eng, count, ring, body):
    with eng.Fori(0, count // ring) as j:
        for r in range(ring):
            body(j * ring + r, r, j)
    for r in range(count % ring):
        body(count // ring * ring + r, r, count // ring)


def row_scale(ve, link, stats, mean, rstd, tmp, act_sqrt):
    qmean, qsq = stats[:, :, :, 1], stats[:, :, :, 2]
    one = lambda k: tmp[:, k, :, 0]
    four = tmp[:, 0:1, :, :].rearrange("p a t q -> p (a t) q")
    link(ve.tensor_reduce(mean, qmean, X, ALU.add))
    link(ve.tensor_scalar(mean, mean, 0.25, None, ALU.mult))
    link(ve.tensor_tensor(four, qmean, mean.unsqueeze(2).broadcast_to([P, NT, 4]), ALU.subtract))
    link(ve.tensor_tensor(four, four, four, ALU.mult))
    link(ve.tensor_reduce(one(1), four, X, ALU.add))
    link(ve.tensor_reduce(one(2), qsq, X, ALU.add))
    link(ve.scalar_tensor_tensor(out=one(1), in0=one(1), scalar=float(D // 4), in1=one(2), op0=ALU.mult, op1=ALU.add))
    link(ve.tensor_scalar(one(1), one(1), 1.0 / D, EPS, ALU.mult, ALU.add))
    act_sqrt(one(1), one(2))
    link(ve.reciprocal(rstd, one(2)))
    link(ve.tensor_tensor(one(2), rstd, rstd, ALU.mult))
    link(ve.tensor_tensor(one(2), one(2), one(1), ALU.mult))
    link(ve.tensor_scalar(one(2), one(2), -0.5, 1.5, ALU.mult, ALU.add))
    link(ve.tensor_tensor(rstd, rstd, one(2), ALU.mult))


def program(nc, a, out):
    ctx = ExitStack()

    def sem(name):
        return ctx.enter_context(nc.semaphore(name))

    def dram(name, shape, dt=F32):
        return nc.dram_tensor(name, shape, dt).ap()

    xt_d = dram("xt_d", [NT, P, D])
    xp_d = dram("xp_d", [NP, D])
    asrc_d = dram("asrc_d", [NP, H])
    smax_d = dram("smax_d", [EP, H])
    first_d = dram("first_d", [EP, 2 * H])
    zsum_d = dram("zsum_d", [EP, H])
    rec_d = dram("rec_d", [EP + EPAD, 8])
    slot_d = dram("slot_d", [2, P * SC], I32)
    xn_d = dram("xn_d", [NP, D])
    tok_d = dram("tok_d", [S2 * P, 2])
    y_d = dram("y_d", [S2 * P, D])
    exp_d = dram("exp_d", [P], I32)

    with ctx:
        def keep(name, shape, dt=F32):
            return ctx.enter_context(nc.sbuf_tensor(name, shape, dt))

        ident = keep("ident", [P, P])
        node_a = keep("node_a", [P, NT, 2 * H])
        eeloop = keep("eeloop", [P, NT, H])
        rz = keep("rz", [P, NT, H])
        iota_all = keep("iota_all", [P, NP])
        before = keep("before", [P, P])
        ones = keep("ones", [P, P])
        pos_i = keep("pos_i", [P, 2, NT], I32)

        with nc.sbuf_tensor("w_sb", [P, KD, D], F32) as w_sb:
            normalise(nc, a, ctx, sem, w_sb, ident, node_a, iota_all, before, ones, xt_d, asrc_d, first_d, tok_d)
            project(nc, a, ctx, sem, w_sb, node_a, eeloop, rz, iota_all, ident, before, ones,
                    xt_d, xp_d, asrc_d, smax_d, first_d, zsum_d, rec_d, slot_d)
        big = keep("big", [P, NT, D])
        sum_edges(nc, a, ctx, sem, big, iota_all, xp_d, rec_d, slot_d)
        route(nc, a, ctx, sem, big, ident, eeloop, rz, before, ones, pos_i, xp_d, xn_d, tok_d, exp_d)
        experts(nc, a, ctx, sem, ident, xn_d, tok_d, exp_d, y_d)
        combine(nc, a, ctx, sem, big, pos_i, y_d, out)


def normalise(nc, a, ctx, sem, w_sb, ident, node_a, iota_all, before, ones, xt_d, asrc_d, first_d, tok_d):
    G = 5
    with ExitStack() as tmp:
        def sb(name, shape, dt=F32):
            return tmp.enter_context(nc.sbuf_tensor(name, shape, dt))

        big = sb("n_x", [P, NT, D])
        att = sb("n_att", [P, 2, D])
        watt = sb("n_watt", [P, KD, 2 * H])
        prod = sb("n_prod", [P, D])
        stats = sb("n_stats", [P, NT, 4, 3])
        mean = sb("n_mean", [P, NT])
        rstd = sb("n_rstd", [P, NT])
        work = sb("n_work", [P, 3, NT, 4])
        xh = sb("n_xh", [P, 2, D])
        xt = sb("n_xt", [P, 2, D])
        zero = sb("n_zero", [P, D])
        ps_t = tmp.enter_context(nc.psum_tensor("n_ps_t", [P, 2, D], F32))
        ps_a = tmp.enter_context(nc.psum_tensor("n_ps_a", [P, 2, 512], F32))

        w_in, att_in = sem("w_in"), sem("att_in")
        x_in = [sem(f"x_in{g}") for g in range(G)]
        consts, zeroed = sem("consts"), sem("zeroed")
        vchain = sem("vchain")
        stats_ready, var_ready, root_ready = sem("stats_ready"), sem("var_ready"), sem("root_ready")
        xh_ready, xt_turned, xt_ready = sem("xh_ready"), sem("xt_turned"), sem("xt_ready")
        xt_out = [sem(f"xt_out{r}") for r in range(2)]
        a_ready, a_done = sem("a_ready"), sem("a_done")
        filled = sem("filled")
        tables_out = sem("tables_out")

        with nc.Block() as block:
            @block.sync
            def _(sp):
                per = NT // G
                for g in range(G):
                    sp.dma_start(big[:, g * per:(g + 1) * per, :],
                                 a["x"][g * per * P:(g + 1) * per * P, :].rearrange("(t p) d -> p t d", p=P)
                                 ).then_inc(x_in[g], 16)
                    if g == 0:
                        sp.dma_start(w_sb[:], a["W"].rearrange("(k p) n -> p k n", p=P)).then_inc(w_in, 16)
                        for j, name in enumerate(("att_src", "att_dst")):
                            sp.dma_start(att[:, j, :], a[name].unsqueeze(0).broadcast_to([P, D])).then_inc(att_in, 16)
                sp.wait_ge(zeroed, 1)
                rows = EP * 2 * H // (P * D)
                sp.dma_start(first_d.rearrange("(q e) c -> q (e c)", q=P)[:, 0:rows * D].rearrange("q (r d) -> q r d", d=D),
                             zero[:].unsqueeze(1).broadcast_to([P, rows, D])).then_inc(filled, 16)
                left = EP * 2 * H // P - rows * D
                sp.dma_start(first_d.rearrange("(q e) c -> q (e c)", q=P)[:, rows * D:rows * D + left],
                             zero[:, 0:left]).then_inc(filled, 16)
                sp.dma_start(tok_d.rearrange("(q e) c -> q (e c)", q=P), zero[:, 0:S2 * 2]).then_inc(filled, 16)

                def store(t, r, j):
                    sp.wait_ge(xt_ready, t + 1 + CREDIT)
                    sp.dma_start(xt_d[ds(t, 1), :, :].rearrange("a p d -> p (a d)"), xt[:, r, :]).then_inc(xt_out[r], 16)
                tiles(sp, NT, 2, store)
                sp.wait_ge(a_done, NT + CREDIT)
                sp.dma_start(asrc_d.rearrange("(t p) h -> p t h", p=P), node_a[:, :, 0:H]).then_inc(tables_out, 16)
                sp.wait_ge(tables_out, 16)
                sp.wait_ge(filled, 48)
                for r in range(2):
                    sp.wait_ge(xt_out[r], 16 * ((NT + 1 - r) // 2))

            @block.gpsimd
            def _(pool):
                pool.memset(zero[:], 0.0).then_inc(zeroed, 1)
                pool.memset(ones[:], 1.0).then_inc(consts, 1)
                pool.iota(iota_all[:], [[1, NP]], base=0, channel_multiplier=0,
                          allow_small_or_imprecise_dtypes=True).then_inc(consts, 1)
                pool.wait_ge(consts, 2)
                pool.affine_select(ident[:], ones[:], [[1, P]], ALU.is_equal, 0.0, base=0, channel_multiplier=-1).then_inc(consts, 1)
                pool.affine_select(before[:], ones[:], [[1, P]], ALU.is_gt, 0.0, base=0, channel_multiplier=-1).then_inc(consts, 1)

            @block.vector
            def _(ve):
                link = Chain(ve, vchain)
                per = NT // G
                for g in range(G):
                    ve.wait_ge(x_in[g], 16)
                    with ve.Fori(g * per, (g + 1) * per) as t:
                        for half in range(2):
                            ve.bn_stats(stats[:, ds(t, 1), 2 * half:2 * half + 2, :].rearrange("p a q s -> p (a q s)"),
                                        big[:, ds(t, 1), half * 512:(half + 1) * 512].rearrange("p a d -> p (a d)")
                                        ).then_inc(stats_ready, 1)
                ve.wait_ge(stats_ready, 2 * NT)

                ve.wait_ge(w_in, 16)
                ve.wait_ge(att_in, 32)
                with ve.Fori(0, KD) as k:
                    def score_columns():
                        for j in range(2):
                            link(ve.tensor_tensor(prod[:], w_sb[:, ds(k, 1), :].rearrange("p a d -> p (a d)"), att[:, j, :], ALU.mult))
                            link(ve.tensor_reduce(watt[:, ds(k, 1), j * H:(j + 1) * H].rearrange("p a h -> p (a h)"),
                                                  prod[:].rearrange("p (h c) -> p h c", h=H), X, ALU.add))
                    link.loop(k, 4, score_columns)
                link.passed(4 * KD)

                def act_sqrt(src, dst):
                    ve.sem_inc(var_ready, 1)
                    ve.wait_ge(root_ready, 1)
                row_scale(ve, link, stats[:], mean[:], rstd[:], work[:], act_sqrt)

                def apply(t, r, j):
                    ve.wait_ge(xt_turned, t + 1)
                    ve.tensor_scalar(xh[:, r, :], big[:, ds(t, 1), :].rearrange("p a d -> p (a d)"),
                                     mean[:, ds(t, 1)], rstd[:, ds(t, 1)], ALU.subtract, ALU.mult).then_inc(xh_ready, 1)
                tiles(ve, NT, 2, apply)

            @block.scalar
            def _(act):
                act.sem_inc(xt_ready, CREDIT)
                act.sem_inc(a_done, CREDIT)
                act.wait_ge(var_ready, 1)
                act.activation(work[:, 2, :, 0], work[:, 1, :, 0], ACT.Sqrt).then_inc(root_ready, 1)

                def evacuate(t, r, j):
                    act.wait_ge(xt_turned, t + 1 + CREDIT)
                    act.wait_ge(a_ready, t + 1)
                    act.wait_ge(xt_out[r], 16 * j)
                    act.copy(xt[:, r, :], ps_t[:, r, :]).then_inc(xt_ready, 1)
                    act.wait_ge(a_ready, t + 1 + CREDIT)
                    act.copy(node_a[:, ds(t, 1), :].rearrange("p a h -> p (a h)"), ps_a[:, r, 0:2 * H]).then_inc(a_done, 1)
                tiles(act, NT, 2, evacuate)

            @block.tensor
            def _(pe):
                pe.sem_inc(xt_turned, CREDIT)
                pe.sem_inc(a_ready, CREDIT)
                pe.wait_ge(consts, 4)

                def turn_and_score(t, r, j):
                    pe.wait_ge(xh_ready, t + 1)
                    pe.wait_ge(xt_ready, t + 1)
                    for k in range(KD):
                        ins = pe.transpose(ps_t[:, r, k * P:(k + 1) * P], xh[:, r, k * P:(k + 1) * P], ident[:])
                    ins.then_inc(xt_turned, 1)
                    pe.wait_ge(xt_ready, t + 1 + CREDIT)
                    pe.wait_ge(a_done, t + 1)
                    for k in range(KD):
                        ins = pe.matmul(ps_a[:, r, 0:2 * H], xt[:, r, k * P:(k + 1) * P], watt[:, k, :],
                                        start=(k == 0), stop=(k == KD - 1))
                    ins.then_inc(a_ready, 1)
                tiles(pe, NT, 2, turn_and_score)


def project(nc, a, ctx, sem, w_sb, node_a, eeloop, rz, iota_all, ident, before, ones,
            xt_d, xp_d, asrc_d, smax_d, first_d, zsum_d, rec_d, slot_d):
    HB = 4
    CT = EC // (HB * KD)
    GB = 16
    assert EC % (HB * KD) == 0 and CT < NT and EC % (2 * GB) == 0
    with ExitStack() as tmp:
        def sb(name, shape, dt=F32):
            return tmp.enter_context(nc.sbuf_tensor(name, shape, dt))

        lt = sb("p_lt", [P, 2, D])
        xp = sb("p_xp", [P, 2, D])
        src_i = sb("p_src", [P, EC], I32)
        dst_i = sb("p_dst", [P, EC], I32)
        prev_i = sb("p_prev", [P, EC], I32)
        part_i = sb("p_part", [P, 2, EC], I32)
        dst_f = sb("p_dst_f", [P, EC])
        hi_lo = sb("p_hi_lo", [P, 2, EC])
        same = sb("p_same", [P, EC])
        cut = sb("p_cut", [P, EC])
        flag4 = sb("p_flag4", [P, 2, H])
        iota_b = sb("p_iota_b", [P, P], BF16)
        zero_b = sb("p_zero_b", [P, P], BF16)
        hot_lo = sb("p_hot_lo", [P, 2, HB, P], BF16)
        hot_hi = sb("p_hot_hi", [P, 2, HB, NT], BF16)
        idx = sb("p_idx", [P, 2, GB], I32)
        got = sb("p_got", [P, 2, GB, H])
        score = sb("p_score", [P, EC, H])
        smax = sb("p_smax", [P, EC, H])
        at_first = sb("p_at_first", [P, EC, 2 * H])
        by_edge = sb("p_by_edge", [P, EC, 2 * H])
        rec = sb("p_rec", [P, EC, 8])
        rec_pad = sb("p_rec_pad", [P, 8])
        deg = sb("p_deg", [P, NT])
        has = sb("p_has", [P, NT])
        t = {n: sb("p_" + n, [P, NT]) for n in
             ("tot", "colbase", "upto", "rowptr", "f0", "slots", "slots_upto", "slots_before", "offset")}
        end_i = sb("p_end_i", [P, NT], I32)
        first_i = sb("p_first_i", [P, NT], I32)
        k_i = sb("p_k_i", [P, NT], I32)
        seg = sb("p_seg", [P, NT, H])
        node_t = sb("p_node_t", [P, NT, 2 * H])
        work = sb("p_work", [P, NT, H])
        s_of = sb("p_s_of", [P, SC])
        hit = sb("p_hit", [P, SC, NT])
        hit2 = sb("p_hit2", [P, SC, NT])
        s_row = sb("p_s_row", [P, 4, SC])
        s_int = sb("p_s_int", [P, 2, SC], I32)
        lasts = sb("p_lasts", [P, H])
        rows = sb("p_rows", [H, 2, P])
        carry = sb("p_carry", [H, P + 1])
        carry_c = sb("p_carry_c", [P, H])
        ps_xp = tmp.enter_context(nc.psum_tensor("p_ps_xp", [P, 2, D], F32))
        ps_deg = tmp.enter_context(nc.psum_tensor("p_ps_deg", [P, 512], F32))
        ps_s = tmp.enter_context(nc.psum_tensor("p_ps_s", [P, 2, 512], F32))

        lt_in = [sem(f"lt_in{r}") for r in range(2)]
        xp_summed, xp_ready = sem("xp_summed"), sem("xp_ready")
        xp_out = [sem(f"xp_out{r}") for r in range(2)]
        edges_in, edges_used = sem("edges_in"), sem("p_consts")
        hot_ready, hot_used = sem("hot_ready"), sem("hot_used")
        vchain = sem("p_vchain")
        idx_ready, got_in = sem("idx_ready"), [sem(f"got_in{r}") for r in range(2)]
        score_ready, pool_passed = sem("score_ready"), sem("pool_passed")
        deg_counted = sem("deg_counted")
        to_pe, from_pe = sem("to_pe"), sem("from_pe")
        smax_ready, smax_out, seg_in = sem("smax_ready"), sem("smax_out"), sem("seg_in")
        node_ready, first_out, first_in = sem("node_ready"), sem("first_out"), sem("first_in")
        exp_ask, exp_done = sem("exp_ask"), sem("exp_done")
        rec_ready, rec_out = sem("rec_ready"), sem("rec_out")
        zs_ready, zs_out, zs_in = sem("zs_ready"), sem("zs_out"), sem("zs_in")
        slot_ready, slot_out = sem("slot_ready"), sem("slot_out")
        edge_major = "(p c) h -> p c h"

        with nc.Block() as block:
            @block.sync
            def _(sp):
                sp.dma_start(dst_i[:], a["dst"][1:1 + EP].rearrange("(p c) -> p c", p=P)).then_inc(edges_in, 16)
                sp.dma_start(prev_i[:], a["dst"][0:EP].rearrange("(p c) -> p c", p=P)).then_inc(edges_in, 16)
                sp.dma_start(src_i[:], a["src"][0:EP].rearrange("(p c) -> p c", p=P)).then_inc(edges_in, 16)

                def load(t, r, j):
                    sp.wait_ge(xp_summed, t + 1)
                    sp.dma_start(lt[:, r, :], xt_d[ds(t, 1), :, :].rearrange("a p d -> p (a d)")).then_inc(lt_in[r], 16)
                tiles(sp, NT, 2, load)

                sp.wait_ge(slot_ready, 1)
                sp.dma_start(slot_d.rearrange("k (p c) -> p k c", p=P), s_int[:]).then_inc(slot_out, 16)
                sp.wait_ge(smax_ready, 1)
                sp.dma_start(smax_d.rearrange(edge_major, p=P), smax[:]).then_inc(smax_out, 16)
                sp.wait_ge(first_out, 16 * NT)
                sp.dma_start(at_first[:], first_d.rearrange(edge_major, p=P)).then_inc(first_in, 16)
                sp.wait_ge(rec_ready, 1)
                sp.dma_start(rec_d[0:EP, :].rearrange(edge_major, p=P), rec[:]).then_inc(rec_out, 16)
                sp.dma_start(rec_d[EP:EP + EPAD, :], rec_pad[:]).then_inc(rec_out, 16)
                sp.wait_ge(zs_ready, 1)
                sp.dma_start(zsum_d.rearrange(edge_major, p=P), smax[:]).then_inc(zs_out, 16)
                sp.wait_ge(rec_out, 32)
                sp.wait_ge(slot_out, 16)

            @block.gpsimd
            def _(pool):
                pool.iota(iota_b[:], [[1, P]], base=0, channel_multiplier=0,
                          allow_small_or_imprecise_dtypes=True).then_inc(edges_used, 1)
                pool.iota(s_of[:], [[1, SC]], base=0, channel_multiplier=SC,
                          allow_small_or_imprecise_dtypes=True).then_inc(edges_used, 1)
                pool.wait_ge(edges_in, 48)

                def gather(j, r, jj):
                    pool.tensor_copy(idx[:, r, :], src_i[:, ds(j * GB, GB)]).then_inc(idx_ready, 1)
                    pool.wait_ge(idx_ready, j + 1)
                    pool.sem_inc(pool_passed, 1)
                    for c in range(GB):
                        pool.indirect_dma_start(got[:, r, c, :], None, asrc_d[:, :],
                                                bass.IndirectOffsetOnAxis(idx[:, r, c:c + 1], 0)).then_inc(got_in[r], 16)

                def keep_scores(j, r, jj):
                    pool.wait_ge(got_in[r], 16 * GB * (jj + 1))
                    pool.tensor_copy(score[:, ds(j * GB, GB), :], got[:, r, :, :]).then_inc(score_ready, 1)
                    pool.wait_ge(score_ready, j + 1)

                passes = EC // GB
                gather(0, 0, 0)
                with pool.Fori(0, passes // 2 - 1) as jj:
                    gather(jj * 2 + 1, 1, jj)
                    keep_scores(jj * 2, 0, jj)
                    gather(jj * 2 + 2, 0, jj + 1)
                    keep_scores(jj * 2 + 1, 1, jj)
                gather(passes - 1, 1, passes // 2 - 1)
                keep_scores(passes - 2, 0, passes // 2 - 1)
                keep_scores(passes - 1, 1, passes // 2 - 1)

                pool.wait_ge(smax_out, 16)
                for n in range(NT):
                    pool.indirect_dma_start(seg[:, n, :], None, smax_d[:, :],
                                            bass.IndirectOffsetOnAxis(end_i[:, n:n + 1], 0)).then_inc(seg_in, 16)
                pool.wait_ge(node_ready, 1)
                for n in range(NT):
                    pool.indirect_dma_start(first_d[:, :], bass.IndirectOffsetOnAxis(first_i[:, n:n + 1], 0),
                                            node_t[:, n, :], None, bounds_check=EP - 1, oob_is_err=False).then_inc(first_out, 16)
                pool.wait_ge(zs_out, 16)
                for n in range(NT):
                    pool.indirect_dma_start(seg[:, n, :], None, zsum_d[:, :],
                                            bass.IndirectOffsetOnAxis(end_i[:, n:n + 1], 0)).then_inc(zs_in, 16)

            @block.vector
            def _(ve):
                link = Chain(ve, vchain)

                def tt(out, x, y, op):
                    link(ve.tensor_tensor(out, x, y, op))

                def ts(out, x, s1, op, s2=None, op2=None):
                    if op2 is None:
                        link(ve.tensor_scalar(out, x, s1, None, op))
                    else:
                        link(ve.tensor_scalar(out, x, s1, s2, op, op2))

                def wide(x, n):
                    return x.unsqueeze(2).broadcast_to([P, x.shape[1], n])

                ve.wait_ge(edges_in, 48)
                ve.wait_ge(edges_used, 2)
                link(ve.memset(zero_b[:], 0.0))
                link(ve.tensor_copy(dst_f[:], dst_i[:]))
                link(ve.tensor_copy(cut[:], prev_i[:]))
                tt(same[:], dst_f[:], cut[:], ALU.is_equal)
                ts(cut[:], same[:], 1.0, ALU.subtract, BIG, ALU.mult)
                for k, flags in enumerate((cut, same)):
                    link(ve.tensor_reduce(lasts[:, 0:1], flags[:], X, ALU.min))
                    link(ve.tensor_copy(flag4[:, k, :], lasts[:, 0:1].broadcast_to([P, H])))
                ts(part_i[:, 0, :], dst_i[:], 7, ALU.arith_shift_right)
                ts(part_i[:, 1, :], dst_i[:], P - 1, ALU.bitwise_and)
                link(ve.tensor_copy(hi_lo[:], part_i[:]))
                ve.sem_inc(to_pe, 1)

                def batch(b, r, j):
                    ve.wait_ge(hot_used, b + 1)
                    for c in range(HB):
                        col = b * HB + c
                        ve.tensor_scalar(hot_lo[:, r, c, :], iota_b[:], hi_lo[:, 1, ds(col, 1)], None, ALU.is_equal)
                        ins = ve.tensor_scalar(hot_hi[:, r, c, :], iota_b[:, 0:NT], hi_lo[:, 0, ds(col, 1)], None, ALU.is_equal)
                    ins.then_inc(hot_ready, 1)
                tiles(ve, EC // HB, 2, batch)

                ve.wait_ge(deg_counted, 1)
                link(ve.tensor_copy(deg[:], ps_deg[:, 0:NT]))
                ve.sem_inc(to_pe, 1)
                ts(has[:], deg[:], 0.0, ALU.is_gt)
                ve.wait_ge(from_pe, 1)
                link(ve.tensor_copy(t["tot"][:], ps_s[:, 1, 0:NT]))
                link(ve.tensor_tensor_scan(t["upto"][:], ones[:, 0:NT], t["tot"][:], 0.0, ALU.mult, ALU.add))
                tt(t["colbase"][:], t["upto"][:], t["tot"][:], ALU.subtract)
                tt(t["rowptr"][:], ps_s[:, 0, 0:NT], t["colbase"][:], ALU.add)
                tt(t["f0"][:], t["rowptr"][:], deg[:], ALU.add)
                ts(t["f0"][:], t["f0"][:], 1.0, ALU.subtract, 0.0, ALU.max)
                link(ve.tensor_copy(end_i[:], t["f0"][:]))
                ts(t["f0"][:], has[:], -float(SKIP), ALU.mult, float(SKIP), ALU.add)
                tt(t["f0"][:], t["f0"][:], t["rowptr"][:], ALU.add)
                link(ve.tensor_copy(first_i[:], t["f0"][:]))

                ts(t["f0"][:], t["tot"][:], float(P - 1), ALU.add)
                link(ve.tensor_copy(k_i[:], t["f0"][:]))
                ts(k_i[:], k_i[:], 7, ALU.arith_shift_right)
                link(ve.tensor_copy(t["slots"][:], k_i[:]))
                link(ve.tensor_tensor_scan(t["slots_upto"][:], ones[:, 0:NT], t["slots"][:], 0.0, ALU.mult, ALU.add))
                tt(t["slots_before"][:], t["slots_upto"][:], t["slots"][:], ALU.subtract)
                link(ve.scalar_tensor_tensor(out=t["offset"][:], in0=t["slots_before"][:], scalar=-float(P),
                                             in1=t["colbase"][:], op0=ALU.mult, op1=ALU.add))
                s_wide = wide(s_of[:], NT)
                over = lambda x: x.unsqueeze(1).broadcast_to([P, SC, NT])
                tt(hit[:], s_wide, over(t["slots_before"][:]), ALU.is_ge)
                tt(hit2[:], s_wide, over(t["slots_upto"][:]), ALU.is_lt)
                tt(hit[:], hit[:], hit2[:], ALU.mult)
                link(ve.tensor_reduce(s_row[:, 0, :], hit[:], X, ALU.add))
                tt(hit2[:], hit[:], over(iota_all[:, 0:NT]), ALU.mult)
                link(ve.tensor_reduce(s_row[:, 1, :], hit2[:], X, ALU.add))
                tt(hit2[:], hit[:], over(t["offset"][:]), ALU.mult)
                link(ve.tensor_reduce(s_row[:, 2, :], hit2[:], X, ALU.add))
                ts(s_row[:, 3, :], s_of[:], float(P), ALU.mult, -float(EP), ALU.add)
                tt(s_row[:, 3, :], s_row[:, 3, :], s_row[:, 0, :], ALU.mult)
                tt(s_row[:, 2, :], s_row[:, 2, :], s_row[:, 3, :], ALU.add)
                ts(s_row[:, 2, :], s_row[:, 2, :], float(EP), ALU.add)
                link(ve.tensor_copy(s_int[:, 0, :], s_row[:, 2, :]))
                link(ve.tensor_copy(s_int[:, 1, :], s_row[:, 1, :]))
                ve.sem_inc(slot_ready, 1)

                asked = [2, 1]

                def segment_scan(out, data, flags, which, op0, op1, initial):
                    for h in range(H):
                        link(ve.tensor_tensor_scan(out[:, :, h], flags[:], data[:, :, h], initial, op0, op1))
                    link(ve.tensor_copy(lasts[:], out[:, EC - 1, :]))
                    ve.sem_inc(to_pe, 1)
                    asked[0] += 1
                    asked[1] += 1
                    ve.wait_ge(from_pe, asked[1])
                    link(ve.tensor_copy(rows[:, 0, :], ps_s[0:H, 0, 0:P]))
                    link(ve.tensor_copy(rows[:, 1, :], ps_s[0:H, 1, 0:P]))
                    link(ve.memset(carry[:, 0:1], initial))
                    link(ve.tensor_tensor_scan(carry[:, 1:P + 1], rows[:, 1, :], rows[:, 0, :], initial, op0, op1))
                    ve.sem_inc(to_pe, 1)
                    asked[0] += 1
                    asked[1] += 1
                    ve.wait_ge(from_pe, asked[1])
                    link(ve.tensor_copy(carry_c[:], ps_s[:, 0, 0:H]))
                    for h in range(H):
                        link(ve.tensor_tensor_scan(out[:, :, h], flags[:], data[:, :, h], carry_c[:, h:h + 1], op0, op1))

                ve.wait_ge(score_ready, EC // GB)
                segment_scan(smax, score, cut, 0, ALU.add, ALU.max, -BIG)
                ve.sem_inc(smax_ready, 1)

                ve.wait_ge(seg_in, 16 * NT)
                has_w = wide(has[:], H)
                a_src, a_dst = node_a[:, :, 0:H], node_a[:, :, H:2 * H]
                tt(seg[:], seg[:], has_w, ALU.mult)
                ts(t["f0"][:], has[:], 1.0, ALU.subtract, BIG, ALU.mult)
                tt(seg[:], seg[:], wide(t["f0"][:], H), ALU.add)
                tt(seg[:], seg[:], a_src, ALU.max)
                tt(seg[:], seg[:], a_dst, ALU.add)
                link(ve.tensor_copy(node_t[:, :, 0:H], a_dst))
                link(ve.scalar_tensor_tensor(out=node_t[:, :, H:2 * H], in0=seg[:], scalar=SLOPE, in1=seg[:],
                                             op0=ALU.mult, op1=ALU.max))
                ve.sem_inc(node_ready, 1)
                tt(work[:], a_src, a_dst, ALU.add)
                link(ve.scalar_tensor_tensor(out=work[:], in0=work[:], scalar=SLOPE, in1=work[:], op0=ALU.mult, op1=ALU.max))
                tt(work[:], work[:], node_t[:, :, H:2 * H], ALU.subtract)
                ve.sem_inc(exp_ask, 1)

                ve.wait_ge(first_in, 16)
                for k in range(2):
                    segment_scan(by_edge[:, :, k * H:(k + 1) * H], at_first[:, :, k * H:(k + 1) * H], same, 1,
                                 ALU.mult, ALU.add, 0.0)
                tt(score[:], score[:], by_edge[:, :, 0:H], ALU.add)
                link(ve.scalar_tensor_tensor(out=score[:], in0=score[:], scalar=SLOPE, in1=score[:], op0=ALU.mult, op1=ALU.max))
                tt(score[:], score[:], by_edge[:, :, H:2 * H], ALU.subtract)
                ts(score[:], score[:], 0.0, ALU.min)
                ve.sem_inc(exp_ask, 1)
                link(ve.memset(rec[:, :, 6:8], 0.0))
                link(ve.tensor_copy(rec[:, :, 0:1].bitcast(I32), src_i[:].unsqueeze(2)))
                link(ve.tensor_copy(rec[:, :, 1:2], dst_f[:].unsqueeze(2)))
                link(ve.memset(rec_pad[:], 0.0))
                link(ve.memset(rec_pad[:, 1:2], float(NO_NODE)))
                ve.wait_ge(exp_done, 2)
                link(ve.tensor_copy(rec[:, :, 2:2 + H], score[:]))
                ve.sem_inc(rec_ready, 1)
                segment_scan(smax, score, same, 1, ALU.mult, ALU.add, 0.0)
                ve.sem_inc(zs_ready, 1)
                ve.wait_ge(zs_in, 16 * NT)
                tt(seg[:], seg[:], has_w, ALU.mult)
                tt(seg[:], seg[:], eeloop[:], ALU.add)
                link(ve.reciprocal(rz[:], seg[:]))

            @block.scalar
            def _(act):
                act.sem_inc(xp_ready, CREDIT)

                def evacuate(t, r, j):
                    act.wait_ge(xp_summed, t + 1 + CREDIT)
                    act.wait_ge(xp_out[r], 16 * j)
                    act.copy(xp[:, r, :], ps_xp[:, r, :]).then_inc(xp_ready, 1)
                    act.wait_ge(xp_ready, t + 1 + CREDIT)
                    act.dma_start(xp_d[ds(t * P, P), :], xp[:, r, :]).then_inc(xp_out[r], 16)
                tiles(act, NT, 2, evacuate)
                act.wait_ge(exp_ask, 1)
                act.activation(eeloop[:], work[:], ACT.Exp).then_inc(exp_done, 1)
                act.wait_ge(exp_ask, 2)
                act.activation(score[:], score[:], ACT.Exp).then_inc(exp_done, 1)
                for r in range(2):
                    act.wait_ge(xp_out[r], 16 * ((NT + 1 - r) // 2))

            @block.tensor
            def _(pe):
                pe.sem_inc(xp_summed, CREDIT)
                pe.sem_inc(hot_used, 2)
                pe.wait_ge(to_pe, 1)
                pe.matmul(ps_deg[:, 0:NT], zero_b[:], zero_b[:, 0:NT], start=True, stop=False)

                def product(t, r, j, count):
                    pe.wait_ge(lt_in[r], 16 * (j + 1))
                    pe.wait_ge(xp_ready, t + 1)
                    for k in range(KD):
                        for half in range(2):
                            ins = pe.matmul(ps_xp[:, r, half * 512:(half + 1) * 512], lt[:, r, k * P:(k + 1) * P],
                                            w_sb[:, k, half * 512:(half + 1) * 512], start=(k == 0), stop=(k == KD - 1))
                        if k == KD - 1:
                            ins.then_inc(xp_summed, 1)
                        if count:
                            b = t * KD + k
                            pe.wait_ge(hot_ready, b + 1)
                            for c in range(HB):
                                ins = pe.matmul(ps_deg[:, 0:NT], hot_lo[:, k % 2, c, :], hot_hi[:, k % 2, c, :],
                                                start=False, stop=False)
                            ins.then_inc(hot_used, 1)

                tiles(pe, CT, 2, lambda t, r, j: product(t, r, j, True))
                pe.matmul(ps_deg[:, 0:NT], zero_b[:], zero_b[:, 0:NT], start=False, stop=True).then_inc(deg_counted, 1)
                assert CT % 2 == 1
                product(CT, 1, CT // 2, False)
                with pe.Fori(0, (NT - CT - 1) // 2) as j:
                    product(j * 2 + CT + 1, 0, j + (CT + 1) // 2, False)
                    product(j * 2 + CT + 2, 1, j + (CT + 1) // 2, False)
                if (NT - CT - 1) % 2:
                    product(NT - 1, 0, NT // 2, False)

                pe.wait_ge(to_pe, 2)
                pe.matmul(ps_s[:, 0, 0:NT], before[:], deg[:], start=True, stop=True)
                pe.matmul(ps_s[:, 1, 0:NT], ones[:], deg[:], start=True, stop=True).then_inc(from_pe, 1)
                for k, which in enumerate((0, 1, 1, 1)):
                    pe.wait_ge(to_pe, 3 + 2 * k)
                    pe.transpose(ps_s[0:H, 0, 0:P], lasts[:], ident[:])
                    pe.transpose(ps_s[0:H, 1, 0:P], flag4[:, which, :], ident[:]).then_inc(from_pe, 1)
                    pe.wait_ge(to_pe, 4 + 2 * k)
                    pe.transpose(ps_s[:, 0, 0:H], carry[:, 0:P], ident[0:H, 0:H]).then_inc(from_pe, 1)


def sum_edges(nc, a, ctx, sem, big, iota_all, xp_d, rec_d, slot_d):
    HR = 4
    with ExitStack() as tmp:
        def sb(name, shape, dt=F32):
            return tmp.enter_context(nc.sbuf_tensor(name, shape, dt))

        table = sb("s_table", [1, 2, P * SC], I32)
        rec = sb("s_rec", [P, U, 8])
        rows = sb("s_rows", [P, U, D])
        hot = sb("s_hot", [P, HR, H, P])
        ps = tmp.enter_context(nc.psum_tensor("s_ps", [P, HR, D], F32))
        table_in, cleared = sem("table_in"), sem("cleared")
        rec_in = [sem(f"rec_in{r}") for r in range(U)]
        rows_in = [sem(f"rows_in{r}") for r in range(U)]
        pool_passed = sem("s_pool_passed")
        hot_ready, summed, added = sem("s_hot_ready"), sem("summed"), sem("added")

        def over_slots(eng, body):
            with eng.Fori(0, S // U) as j:
                body(j)

        with nc.Block() as block:
            @block.sync
            def _(sp):
                sp.dma_start(table[:], slot_d.unsqueeze(0)).then_inc(table_in, 16)
                sp.wait_ge(table_in, 16)

                def body(j):
                    first = nc.values_load_multi_w_load_instructions(
                        table[0:1, 0, ds(j * U, U)], engines=(mybir.EngineType.SP,), min_val=0, max_val=EP,
                        skip_runtime_bounds_check_because="starts are within the edges")[1]
                    for r in range(U):
                        sp.wait_ge(summed, j * U + r + 1)
                        sp.dma_start(rec[:, r, :], rec_d[ds(first[r], P), :]).then_inc(rec_in[r], 16)
                over_slots(sp, body)

            @block.gpsimd
            def _(pool):
                def body(j):
                    for r in range(U):
                        pool.wait_ge(rec_in[r], 16 * (j + 1))
                        pool.wait_ge(summed, j * U + r + 1)
                        pool.sem_inc(pool_passed, 1)
                        pool.indirect_dma_start(rows[:, r, :], None, xp_d[:, :],
                                                bass.IndirectOffsetOnAxis(rec[:, r, 0:1].bitcast(I32), 0)
                                                ).then_inc(rows_in[r], 16)
                over_slots(pool, body)

            @block.vector
            def _(ve):
                ve.sem_inc(added, HR)
                ve.wait_ge(table_in, 16)
                ve.memset(big[:], 0.0).then_inc(cleared, 1)
                ve.wait_ge(cleared, 1)

                def load_tiles(s, n):
                    return nc.values_load_multi_w_load_instructions(
                        table[0:1, 1, ds(s, n)], engines=(mybir.EngineType.DVE,), min_val=0, max_val=NT - 1,
                        skip_runtime_bounds_check_because="node tiles")[1]

                def weigh(s, r, j, tile):
                    ve.wait_ge(rec_in[r], 16 * (j + 1))
                    ve.wait_ge(summed, s + 1 + U - HR)
                    for h in range(H):
                        ins = ve.tensor_scalar(hot[:, r % HR, h, :], iota_all[:, ds(tile * P, P)], rec[:, r, 1:2],
                                               rec[:, r, 2 + h:3 + h], ALU.is_equal, ALU.mult)
                    ins.then_inc(hot_ready, 1)

                def add(s, r, tile):
                    ve.wait_ge(summed, s + 1 + U)
                    ve.wait_ge(added, s + HR)
                    node = big[:, ds(tile, 1), :].rearrange("p a d -> p (a d)")
                    ve.tensor_tensor(node, node, ps[:, r % HR, :], ALU.add).then_inc(added, 1)

                def body(j, last):
                    tile = load_tiles(j * U, U if last else U + AHEAD)
                    for r in range(U):
                        s, q = j * U + r, r + AHEAD
                        if not (last and q >= U):
                            weigh(s + AHEAD, q % U, j + q // U, tile[q])
                        add(s, r, tile[r])

                tile = load_tiles(0, AHEAD)
                for r in range(AHEAD):
                    weigh(r, r, 0, tile[r])
                with ve.Fori(0, S // U - 1) as j:
                    body(j, False)
                body(S // U - 1, True)

            @block.tensor
            def _(pe):
                pe.sem_inc(summed, U)

                def body(j):
                    for r in range(U):
                        s = j * U + r
                        pe.wait_ge(hot_ready, s + 1)
                        pe.wait_ge(rows_in[r], 16 * (j + 1))
                        pe.wait_ge(added, s + 1)
                        for h in range(H):
                            ins = pe.matmul(ps[:, r % HR, h * C:(h + 1) * C], hot[:, r % HR, h, :],
                                            rows[:, r, h * C:(h + 1) * C], start=True, stop=True)
                        ins.then_inc(summed, 1)
                over_slots(pe, body)


def route(nc, a, ctx, sem, big, ident, eeloop, rz, before, ones, pos_i, xp_d, xn_d, tok_d, exp_d):
    with ExitStack() as tmp:
        def sb(name, shape, dt=F32):
            return tmp.enter_context(nc.sbuf_tensor(name, shape, dt))

        bias = sb("r_bias", [P, D])
        proj = sb("r_proj", [P, KD, NE])
        anchors = sb("r_anchors", [P, NE * NE])
        temp = sb("r_temp", [P, 1])
        xp = sb("r_xp", [P, 2, D])
        xin = sb("r_xin", [P, 2, D])
        stats = sb("r_stats", [P, NT, 4, 3])
        mean = sb("r_mean", [P, NT])
        rstd = sb("r_rstd", [P, NT])
        work = sb("r_work", [P, 3, NT, 4])
        xh = sb("r_xh", [P, 2, D])
        xt = sb("r_xt", [P, 2, D])
        t6 = {n: sb("r_" + n, [P, NT, NE]) for n in
              ("z", "q", "logit", "tmp", "rank", "ex", "sel", "w", "tot", "upto", "pos")}
        top = sb("r_top", [P, NT])
        e1 = {n: sb("r_" + n, [P, NE]) for n in ("cnt", "slots", "slots_upto", "slots_before")}
        k_i = sb("r_k_i", [P, NE], I32)
        slot_no = sb("r_slot_no", [P, 1])
        expert = sb("r_expert", [P, 1])
        expert_i = sb("r_expert_i", [P, 1], I32)
        token_no = sb("r_token_no", [P, NT], I32)
        tok = sb("r_tok", [P, 2, NT, 2])
        ps_t = tmp.enter_context(nc.psum_tensor("r_ps_t", [P, 2, D], F32))
        ps_z = tmp.enter_context(nc.psum_tensor("r_ps_z", [P, 2, 512], F32))

        small_in = sem("small_in")
        row_in = [sem(f"row_in{r}") for r in range(2)]
        vchain, rchain = sem("r_vchain"), sem("r_rows_chain")
        stats_ready, var_ready, root_ready = sem("r_stats_ready"), sem("r_var_ready"), sem("r_root_ready")
        xh_ready, xt_turned, xt_ready = sem("r_xh_ready"), sem("r_xt_turned"), sem("r_xt_ready")
        xn_out = [sem(f"xn_out{r}") for r in range(2)]
        z_summed, z_ready = sem("z_summed"), sem("z_ready")
        act_ask, act_done = sem("r_act_ask"), sem("r_act_done")
        to_pe, from_pe = sem("r_to_pe"), sem("r_from_pe")
        consts = sem("r_consts")
        tok_ready, tok_out, exp_ready, exp_out = sem("tok_ready"), sem("tok_out"), sem("exp_ready"), sem("exp_out")
        STEPS = 2 * H + 1

        with nc.Block() as block:
            @block.sync
            def _(sp):
                sp.dma_start(bias[:], a["bias"].unsqueeze(0).broadcast_to([P, D])).then_inc(small_in, 16)
                sp.dma_start(proj[:], a["proj_t"].rearrange("(k p) e -> p k e", p=P)).then_inc(small_in, 16)
                sp.dma_start(anchors[:], a["anchors"].unsqueeze(0).broadcast_to([P, NE * NE])).then_inc(small_in, 16)
                sp.dma_start(temp[:], a["temp"].unsqueeze(0).broadcast_to([P, 1])).then_inc(small_in, 16)

                def load(t, r, j):
                    sp.wait_ge(rchain, STEPS * (t + 1))
                    sp.dma_start(xp[:, r, :], xp_d[ds(t * P, P), :]).then_inc(row_in[r], 16)
                    sp.dma_start(xin[:, r, :], a["x"][ds(t * P, P), :]).then_inc(row_in[r], 16)
                tiles(sp, NT, 2, load)

                def store(t, r, j):
                    sp.wait_ge(xh_ready, t + 1)
                    sp.dma_start(xn_d[ds(t * P, P), :], xh[:, r, :]).then_inc(xn_out[r], 16)
                tiles(sp, NT, 2, store)
                for r in range(2):
                    sp.wait_ge(xn_out[r], 16 * ((NT + 1 - r) // 2))
                sp.wait_ge(exp_ready, 1)
                sp.dma_start(exp_d.unsqueeze(1), expert_i[:]).then_inc(exp_out, 16)
                sp.wait_ge(exp_out, 16)

            @block.gpsimd
            def _(pool):
                pool.iota(slot_no[:], [[0, 1]], base=0, channel_multiplier=1,
                          allow_small_or_imprecise_dtypes=True).then_inc(consts, 1)
                pool.iota(token_no[:], [[P, NT]], base=0, channel_multiplier=1).then_inc(consts, 1)
                pool.wait_ge(tok_ready, 1)
                for k in range(2):
                    for t in range(NT):
                        pool.indirect_dma_start(tok_d[:, :], bass.IndirectOffsetOnAxis(pos_i[:, k, t:t + 1], 0),
                                                tok[:, k, t, :], None).then_inc(tok_out, 16)
                pool.wait_ge(tok_out, 16 * 2 * NT)

            @block.vector
            def _(ve):
                rows = Chain(ve, rchain)
                ve.sem_inc(rchain, 2 * STEPS)
                rows.n = 2 * STEPS
                ve.wait_ge(small_in, 64)

                def layer_rows(t, r, j):
                    ve.wait_ge(row_in[r], 32 * (j + 1))
                    x1 = big[:, ds(t, 1), :].rearrange("p a d -> p (a d)")

                    def steps():
                        for h in range(H):
                            c = slice(h * C, (h + 1) * C)
                            rows(ve.scalar_tensor_tensor(out=x1[:, c], in0=xp[:, r, c], scalar=eeloop[:, ds(t, 1), h],
                                                         in1=x1[:, c], op0=ALU.mult, op1=ALU.add))
                            rows(ve.scalar_tensor_tensor(out=x1[:, c], in0=x1[:, c], scalar=rz[:, ds(t, 1), h],
                                                         in1=bias[:, c], op0=ALU.mult, op1=ALU.add))
                        rows(ve.scalar_tensor_tensor(out=x1, in0=x1, scalar=0.0, in1=xin[:, r, :], op0=ALU.max, op1=ALU.add))
                    rows.loop(t, STEPS, steps)
                    for half in range(2):
                        ve.bn_stats(stats[:, ds(t, 1), 2 * half:2 * half + 2, :].rearrange("p a q s -> p (a q s)"),
                                    x1[:, half * 512:(half + 1) * 512]).then_inc(stats_ready, 1)
                tiles(ve, NT, 2, layer_rows)
                ve.wait_ge(stats_ready, 2 * NT)
                link = Chain(ve, vchain)

                def act_sqrt(src, dst):
                    ve.sem_inc(var_ready, 1)
                    ve.wait_ge(root_ready, 1)
                row_scale(ve, link, stats[:], mean[:], rstd[:], work[:], act_sqrt)

                def apply(t, r, j):
                    ve.wait_ge(xt_turned, t + 1)
                    ve.wait_ge(xn_out[r], 16 * j)
                    ve.tensor_scalar(xh[:, r, :], big[:, ds(t, 1), :].rearrange("p a d -> p (a d)"),
                                     mean[:, ds(t, 1)], rstd[:, ds(t, 1)], ALU.subtract, ALU.mult).then_inc(xh_ready, 1)
                tiles(ve, NT, 2, apply)

                def tt(out, x, y, op):
                    link(ve.tensor_tensor(out, x, y, op))

                def ts(out, x, s1, op, s2=None, op2=None):
                    if op2 is None:
                        link(ve.tensor_scalar(out, x, s1, None, op))
                    else:
                        link(ve.tensor_scalar(out, x, s1, s2, op, op2))

                def each_expert(x):
                    return x.unsqueeze(2).broadcast_to([P, NT, NE])

                def each_tile(x):
                    return x.unsqueeze(1).broadcast_to([P, NT, NE])

                z, q, logit, tm, rank, ex, sel, w, tot, upto, pos = (
                    t6[n][:] for n in ("z", "q", "logit", "tmp", "rank", "ex", "sel", "w", "tot", "upto", "pos"))
                ve.wait_ge(z_ready, NT + CREDIT)
                ve.sem_inc(act_ask, 1)
                ts(temp[:], temp[:], 0.1, ALU.max)
                link(ve.reciprocal(temp[:], temp[:]))
                for e in range(NE):
                    link(ve.memset(rank[:, :, e], float(NE - 1 - e)))
                link(ve.memset(logit, 0.0))
                ve.wait_ge(act_done, 1)
                anchor = anchors[:].rearrange("p (f e) -> p f e", e=NE)
                for e in range(NE):
                    tt(tm, each_expert(q[:, :, e]), each_tile(anchor[:, :, e]), ALU.mult)
                    tt(logit, logit, tm, ALU.add)
                ts(logit, logit, float(NE), ALU.subtract, 0.5, ALU.mult)
                ts(logit, logit, temp[:], ALU.mult)
                for i in range(NE):
                    for k in range(i + 1, NE):
                        tt(top[:], logit[:, :, i], logit[:, :, k], ALU.is_ge)
                        tt(rank[:, :, i], rank[:, :, i], top[:], ALU.subtract)
                        tt(rank[:, :, k], rank[:, :, k], top[:], ALU.add)
                link(ve.tensor_reduce(top[:], logit, X, ALU.max))
                tt(ex, logit, each_expert(top[:]), ALU.subtract)
                ve.sem_inc(act_ask, 1)
                ts(sel, rank, 1.5, ALU.is_lt)
                ve.sem_inc(to_pe, 1)
                ve.wait_ge(act_done, 2)
                tt(w, ex, sel, ALU.mult)
                link(ve.tensor_reduce(top[:], w, X, ALU.add))
                link(ve.reciprocal(top[:], top[:]))
                tt(w, w, each_expert(top[:]), ALU.mult)
                ve.wait_ge(from_pe, 1)
                link(ve.tensor_copy(tot.rearrange("p t e -> p (t e)"), ps_z[:, 1, 0:NT * NE]))
                link(ve.tensor_copy(pos.rearrange("p t e -> p (t e)"), ps_z[:, 0, 0:NT * NE]))
                for e in range(NE):
                    link(ve.tensor_tensor_scan(upto[:, :, e], ones[:, 0:NT], tot[:, :, e], 0.0, ALU.mult, ALU.add))
                tt(pos, pos, upto, ALU.add)
                tt(pos, pos, tot, ALU.subtract)
                ts(e1["cnt"][:], upto[:, NT - 1, :], float(P - 1), ALU.add)
                link(ve.tensor_copy(k_i[:], e1["cnt"][:]))
                ts(k_i[:], k_i[:], 7, ALU.arith_shift_right)
                link(ve.tensor_copy(e1["slots"][:], k_i[:]))
                link(ve.tensor_tensor_scan(e1["slots_upto"][:], ones[:, 0:NE], e1["slots"][:], 0.0, ALU.mult, ALU.add))
                tt(e1["slots_before"][:], e1["slots_upto"][:], e1["slots"][:], ALU.subtract)
                ts(e1["slots_before"][:], e1["slots_before"][:], float(P), ALU.mult)
                tt(pos, pos, each_tile(e1["slots_before"][:]), ALU.add)
                ve.wait_ge(consts, 2)
                ts(e1["cnt"][:, 0:NE - 1], e1["slots_upto"][:, 0:NE - 1], slot_no[:], ALU.is_le)
                link(ve.tensor_reduce(expert[:], e1["cnt"][:, 0:NE - 1], X, ALU.add))
                link(ve.tensor_copy(expert_i[:], expert[:]))
                ve.sem_inc(exp_ready, 1)
                for k in range(2):
                    ts(sel, rank, float(k), ALU.is_equal)
                    tt(tm, sel, pos, ALU.mult)
                    link(ve.tensor_reduce(top[:], tm, X, ALU.add))
                    link(ve.tensor_copy(pos_i[:, k, :], top[:]))
                    tt(tm, sel, w, ALU.mult)
                    link(ve.tensor_reduce(tok[:, k, :, 1], tm, X, ALU.add))
                    link(ve.tensor_copy(tok[:, k, :, 0:1].bitcast(I32), token_no[:].unsqueeze(2)))
                ve.sem_inc(tok_ready, 1)

            @block.scalar
            def _(act):
                act.sem_inc(xt_ready, CREDIT)
                act.sem_inc(z_ready, CREDIT)
                act.wait_ge(var_ready, 1)
                act.activation(work[:, 2, :, 0], work[:, 1, :, 0], ACT.Sqrt).then_inc(root_ready, 1)

                def evacuate(t, r, j):
                    act.wait_ge(xt_turned, t + 1 + CREDIT)
                    act.wait_ge(z_summed, t + 1)
                    act.copy(xt[:, r, :], ps_t[:, r, :]).then_inc(xt_ready, 1)
                    act.wait_ge(z_summed, t + 1 + CREDIT)
                    act.copy(t6["z"][:, ds(t, 1), :].rearrange("p a e -> p (a e)"), ps_z[:, r, 0:NE]).then_inc(z_ready, 1)
                tiles(act, NT, 2, evacuate)
                act.wait_ge(act_ask, 1)
                act.activation(t6["q"][:], t6["z"][:], ACT.Tanh, scale=1.0 / QUANT_TEMP).then_inc(act_done, 1)
                act.wait_ge(act_ask, 2)
                act.activation(t6["ex"][:], t6["ex"][:], ACT.Exp).then_inc(act_done, 1)

            @block.tensor
            def _(pe):
                pe.sem_inc(xt_turned, CREDIT)
                pe.sem_inc(z_summed, CREDIT)
                pe.wait_ge(small_in, 64)

                def turn_and_multiply(t, r, j):
                    pe.wait_ge(xh_ready, t + 1)
                    pe.wait_ge(xt_ready, t + 1)
                    for k in range(KD):
                        ins = pe.transpose(ps_t[:, r, k * P:(k + 1) * P], xh[:, r, k * P:(k + 1) * P], ident[:])
                    ins.then_inc(xt_turned, 1)
                    pe.wait_ge(xt_ready, t + 1 + CREDIT)
                    pe.wait_ge(z_ready, t + 1)
                    for k in range(KD):
                        ins = pe.matmul(ps_z[:, r, 0:NE], xt[:, r, k * P:(k + 1) * P], proj[:, k, :],
                                        start=(k == 0), stop=(k == KD - 1))
                    ins.then_inc(z_summed, 1)
                tiles(pe, NT, 2, turn_and_multiply)
                pe.wait_ge(to_pe, 1)
                chosen = t6["sel"][:].rearrange("p t e -> p (t e)")
                pe.matmul(ps_z[:, 0, 0:NT * NE], before[:], chosen, start=True, stop=True)
                pe.matmul(ps_z[:, 1, 0:NT * NE], ones[:], chosen, start=True, stop=True).then_inc(from_pe, 1)


def experts(nc, a, ctx, sem, ident, xn_d, tok_d, exp_d, y_d):
    assert S2 % 2 == 0
    with ExitStack() as tmp:
        def sb(name, shape, dt=F32):
            return tmp.enter_context(nc.sbuf_tensor(name, shape, dt))

        table = sb("e_table", [1, P], I32)
        tok = sb("e_tok", [P, S2, 2])
        w1 = sb("e_w1", [P, 2, KD, DH])
        w2 = sb("e_w2", [P, 2, KH, D])
        idx = sb("e_idx", [P, 2], I32)
        xg = sb("e_xg", [P, 2, D])
        xt = sb("e_xt", [P, D])
        hid = sb("e_hid", [P, DH])
        hidt = sb("e_hidt", [P, DH])
        y = sb("e_y", [P, 2, D])
        ps_t = tmp.enter_context(nc.psum_tensor("e_ps_t", [P, D], F32))
        ps_h = tmp.enter_context(nc.psum_tensor("e_ps_h", [P, DH], F32))
        ps_ht = tmp.enter_context(nc.psum_tensor("e_ps_ht", [P, DH], F32))
        ps_y = tmp.enter_context(nc.psum_tensor("e_ps_y", [P, 2, D], F32))

        tables_in = sem("e_tables_in")
        w_in = [sem(f"e_w_in{r}") for r in range(2)]
        xg_in = [sem(f"xg_in{r}") for r in range(2)]
        y_out = [sem(f"y_out{r}") for r in range(2)]
        idx_ready, pool_passed = sem("e_idx_ready"), sem("e_pool_passed")
        turned, xt_ready, h_summed, h_ready = sem("turned"), sem("e_xt_ready"), sem("h_summed"), sem("h_ready")
        h_turned, ht_ready, y_summed, y_ready = sem("h_turned"), sem("ht_ready"), sem("y_summed"), sem("y_ready")

        with nc.Block() as block:
            @block.sync
            def _(sp):
                sp.dma_start(table[:], exp_d.unsqueeze(0)).then_inc(tables_in, 16)
                sp.dma_start(tok[:], tok_d.rearrange("(s p) c -> p s c", p=P)).then_inc(tables_in, 16)
                sp.wait_ge(tables_in, 32)

                def load(s, r, j):
                    e = sp.value_load(table[0:1, ds(s, 1)], min_val=0, max_val=NE - 1)
                    sp.wait_ge(y_summed, s + 1)
                    sp.dma_start(w1[:, r, :, :], a["w1"][ds(e, 1), :, :].rearrange("a (k p) h -> p (a k) h", p=P)).then_inc(w_in[r], 16)
                    sp.dma_start(w2[:, r, :, :], a["w2"][ds(e, 1), :, :].rearrange("a (k p) d -> p (a k) d", p=P)).then_inc(w_in[r], 16)
                tiles(sp, S2, 2, load)

            @block.gpsimd
            def _(pool):
                pool.wait_ge(tables_in, 32)

                def gather(s, r, j):
                    pool.wait_ge(turned, s + 1)
                    pool.tensor_copy(idx[:, r:r + 1], tok[:, ds(s, 1), 0].bitcast(I32)).then_inc(idx_ready, 1)
                    pool.wait_ge(idx_ready, s + 1)
                    pool.sem_inc(pool_passed, 1)
                    pool.indirect_dma_start(xg[:, r, :], None, xn_d[:, :],
                                            bass.IndirectOffsetOnAxis(idx[:, r:r + 1], 0)).then_inc(xg_in[r], 16)
                tiles(pool, S2, 2, gather)

            @block.tensor
            def _(pe):
                pe.sem_inc(turned, CREDIT)
                pe.sem_inc(y_summed, CREDIT)

                def turn(s, r, j):
                    pe.wait_ge(xg_in[r], 16 * (j + 1))
                    pe.wait_ge(xt_ready, s)
                    for k in range(KD):
                        ins = pe.transpose(ps_t[:, k * P:(k + 1) * P], xg[:, r, k * P:(k + 1) * P], ident[:])
                    ins.then_inc(turned, 1)

                def slot(s, r, j, last):
                    pe.wait_ge(w_in[r], 32 * (j + 1))
                    pe.wait_ge(xt_ready, s + 1)
                    pe.wait_ge(h_ready, s)
                    for k in range(KD):
                        ins = pe.matmul(ps_h[:], xt[:, k * P:(k + 1) * P], w1[:, r, k, :], start=(k == 0), stop=(k == KD - 1))
                    ins.then_inc(h_summed, 1)
                    if not last:
                        turn(s + 1, 1 - r, j + r)
                    pe.wait_ge(h_ready, s + 1)
                    pe.wait_ge(ht_ready, s)
                    for k in range(KH):
                        ins = pe.transpose(ps_ht[:, k * P:(k + 1) * P], hid[:, k * P:(k + 1) * P], ident[:])
                    ins.then_inc(h_turned, 1)
                    pe.wait_ge(ht_ready, s + 1)
                    pe.wait_ge(y_ready, s + 1)
                    for k in range(KH):
                        for half in range(2):
                            ins = pe.matmul(ps_y[:, r, half * 512:(half + 1) * 512], hidt[:, k * P:(k + 1) * P],
                                            w2[:, r, k, half * 512:(half + 1) * 512], start=(k == 0), stop=(k == KH - 1))
                    ins.then_inc(y_summed, 1)

                turn(0, 0, 0)
                with pe.Fori(0, S2 // 2 - 1) as j:
                    for r in range(2):
                        slot(j * 2 + r, r, j, False)
                slot(S2 - 2, 0, S2 // 2 - 1, False)
                slot(S2 - 1, 1, S2 // 2 - 1, True)

            @block.scalar
            def _(act):
                def keep_turned(s):
                    act.wait_ge(turned, s + 1 + CREDIT)
                    act.wait_ge(h_summed, s)
                    act.copy(xt[:], ps_t[:]).then_inc(xt_ready, 1)

                def slot(s, last):
                    act.wait_ge(h_summed, s + 1)
                    act.wait_ge(h_turned, s)
                    act.activation(hid[:], ps_h[:], ACT.Gelu_apprx_tanh).then_inc(h_ready, 1)
                    if not last:
                        keep_turned(s + 1)

                def store(s, r):
                    act.wait_ge(y_ready, s + 1 + CREDIT)
                    act.dma_start(y_d[ds(s * P, P), :], y[:, r, :]).then_inc(y_out[r], 16)

                keep_turned(0)
                slot(0, False)
                with act.Fori(0, S2 // 2 - 1) as j:
                    for r in range(2):
                        slot(j * 2 + 1 + r, False)
                        store(j * 2 + r, r)
                slot(S2 - 1, True)
                store(S2 - 2, 0)
                store(S2 - 1, 1)

            @block.vector
            def _(ve):
                ve.sem_inc(y_ready, CREDIT)
                ve.wait_ge(tables_in, 32)

                def slot(s, r, j):
                    ve.wait_ge(h_turned, s + 1)
                    ve.wait_ge(y_summed, s + 1 + CREDIT - 1)
                    ve.tensor_copy(hidt[:], ps_ht[:]).then_inc(ht_ready, 1)
                    ve.wait_ge(y_summed, s + 1 + CREDIT)
                    ve.wait_ge(y_out[r], 16 * j)
                    ve.tensor_scalar(y[:, r, :], ps_y[:, r, :], tok[:, ds(s, 1), 1], None, ALU.mult).then_inc(y_ready, 1)
                tiles(ve, S2, 2, slot)

            @block.sync
            def _(sp):
                for r in range(2):
                    sp.wait_ge(y_out[r], 16 * (S2 // 2))


def combine(nc, a, ctx, sem, big, pos_i, y_d, out):
    with ExitStack() as tmp:
        def sb(name, shape, dt=F32):
            return tmp.enter_context(nc.sbuf_tensor(name, shape, dt))

        R = 4
        idx = sb("c_idx", [P, R, 2], I32)
        got = sb("c_got", [P, R, 2, D])
        o = sb("c_o", [P, R, D])
        idx_ready, pool_passed = sem("c_idx_ready"), sem("c_pool_passed")
        got_in = [sem(f"c_got_in{r}") for r in range(R)]
        o_out = [sem(f"o_out{r}") for r in range(R)]
        o_half, o_ready = sem("o_half"), sem("o_ready")

        with nc.Block() as block:
            @block.gpsimd
            def _(pool):
                def gather(t, r, j):
                    pool.wait_ge(o_ready, t + 1)
                    pool.tensor_copy(idx[:, r, :], pos_i[:, :, ds(t, 1)].rearrange("p k a -> p (k a)")).then_inc(idx_ready, 1)
                    pool.wait_ge(idx_ready, t + 1)
                    pool.sem_inc(pool_passed, 1)
                    for k in range(2):
                        pool.indirect_dma_start(got[:, r, k, :], None, y_d[:, :],
                                                bass.IndirectOffsetOnAxis(idx[:, r, k:k + 1], 0)).then_inc(got_in[r], 16)
                tiles(pool, NT, R, gather)

            @block.vector
            def _(ve):
                ve.sem_inc(o_ready, R)

                def add(t, r, j):
                    ve.wait_ge(got_in[r], 32 * (j + 1))
                    ve.wait_ge(o_out[r], 16 * j)
                    ve.tensor_tensor(o[:, r, :], got[:, r, 0, :], got[:, r, 1, :], ALU.add).then_inc(o_half, 1)
                    ve.wait_ge(o_half, t + 1)
                    ve.tensor_tensor(o[:, r, :], o[:, r, :], big[:, ds(t, 1), :].rearrange("p a d -> p (a d)"),
                                     ALU.add).then_inc(o_ready, 1)
                tiles(ve, NT, R, add)

            @block.sync
            def _(sp):
                def store(t, r, j):
                    sp.wait_ge(o_ready, t + 1 + R)
                    sp.dma_start(out[ds(t * P, P), :], o[:, r, :]).then_inc(o_out[r], 16)
                tiles(sp, NT, R, store)
                for r in range(R):
                    sp.wait_ge(o_out[r], 16 * ((NT + R - 1 - r) // R))


def kernel(**inputs):
    import concourse.bacc as bacc
    from concourse.bass_utils import run_bass_kernel_spmd

    def padded(v, rows, value=0):
        return np.concatenate([v, np.full((rows - v.shape[0],) + v.shape[1:], value, v.dtype)])

    g = {k: np.asarray(v) for k, v in inputs.items()}
    none = np.full((1,), NO_NODE, np.int32)
    arrays = {
        "x": padded(g["x"], NP),
        "src": padded(g["src"], EP + EPAD),
        "dst": np.concatenate([none, padded(g["dst"], EP + EPAD, NO_NODE)]),
        "W": g["L0_gnn_W"],
        "att_src": g["L0_gnn_att_src"].reshape(D),
        "att_dst": g["L0_gnn_att_dst"].reshape(D),
        "bias": g["L0_gnn_bias"],
        "proj_t": g["L0_ffn_proj_w"].T,
        "anchors": g["L0_ffn_anchors"].reshape(NE * NE),
        "temp": g["L0_ffn_routing_temp"].reshape(1),
        "w1": g["L0_ffn_w1"],
        "w2": g["L0_ffn_w2"],
    }
    arrays = {k: np.ascontiguousarray(v) for k, v in arrays.items()}
    nc = bacc.Bacc("TRN2", target_bir_lowering=False, num_devices=1)
    a = {k: nc.dram_tensor(f"in_{k}", v.shape, mybir.dt.from_np(v.dtype), kind="ExternalInput").ap()
         for k, v in arrays.items()}
    out = nc.dram_tensor("out_rows", (NP, D), F32, kind="ExternalOutput").ap()
    program(nc, a, out)
    r = run_bass_kernel_spmd(nc, [{f"in_{k}": v for k, v in arrays.items()}], core_ids=[0])
    return r.results[0]["out_rows"][:N]
```
